# Optimizing a Trainium2 kernel written in Bass

```python
import numpy as np
import jax
import jax.numpy as jnp

def _softmax(x, axis=-1):
    return jax.nn.softmax(x, axis=axis)

def _gelu(x):
    return jax.nn.gelu(x, approximate=True)

def _silu(x):
    return jax.nn.silu(x)

def _sigmoid(x):
    return jax.nn.sigmoid(x)

def _layernorm(x, axis=-1, eps=1e-05):
    m = jnp.mean(x, axis=axis, keepdims=True)
    v = jnp.var(x, axis=axis, keepdims=True)
    return (x - m) / jnp.sqrt(v + eps)

def _scatter_add(tgt, idx, src, axis=0):
    return tgt.at[idx].add(src)

def _segment_sum(src, seg, n):
    return jax.ops.segment_sum(src, seg, n)
kernel_name = 'mk_cond_resid_d1_seqx_r2_a8e0ed'

def setup_inputs(seed: int=0):
    np.random.seed(seed)
    _w = jnp.asarray

    def _rec_inputs():
        import jax
        import jax.numpy as jnp
        _rk = jax.random.key(seed)
        x = -0.0001546 + 1 * jax.random.normal(jax.random.fold_in(_rk, 1), (8, 512, 512), jnp.float32)
        _lenS = 512 - jax.random.randint(jax.random.fold_in(_rk, 7), (8,), 0, max(1, 512 // 4) + 1, jnp.int32)
        _lenS2 = 512 - jax.random.randint(jax.random.fold_in(_rk, 8), (8,), 0, max(1, 512 // 4) + 1, jnp.int32)
        itok_B_1_98 = jax.random.randint(jax.random.fold_in(_rk, 11), (8,), 1, 99, jnp.int32)
        return (x, itok_B_1_98)
    x, itok_B_1_98 = _rec_inputs()

    def _L0_cond_setup():
        import jax, jax.numpy as jnp
        import numpy as np
        B = 128
        D = 512
        K = 100
        key = jax.random.key(seed)
        kx, kt, ks = jax.random.split(key, 3)
        x = jax.random.normal(kx, (B, D, D), dtype=jnp.float32)
        T = jax.random.normal(kt, (K, D, D), dtype=jnp.float32)
        fwd_steps = jax.random.randint(ks, (B,), 1, K + 1, dtype=jnp.int64)
        return {'x': x, 'fwd_steps': fwd_steps, 'T': T}
    _L0_cond_all = _L0_cond_setup()
    _L0_cond_in = {k: v for k, v in _L0_cond_all.items() if k in ('T',)}
    del _L0_cond_all
    return {'x': x, 'itok_B_1_98': itok_B_1_98, 'L0_cond_T': _L0_cond_in['T']}

def reference(x, itok_B_1_98, L0_cond_T):
    import jax
    import jax.numpy as jnp

    def _L0_cond_ref(x, fwd_steps, T):
        import jax, jax.numpy as jnp
        import numpy as np
        B = 128
        D = 512
        K = 100
        Tb = T[fwd_steps - 1]
        return jnp.einsum('bij,bjk->bik', Tb, x)
    x = x + _L0_cond_ref(x, itok_B_1_98, L0_cond_T)
    return x

_drawn_inputs = setup_inputs


def setup_inputs(seed=0):
    import zlib

    import numpy as np

    out = dict(_drawn_inputs(seed))
    spreads = {}
    factors = {}
    for name, (base, spread) in spreads.items():
        noise = np.random.default_rng([zlib.crc32(name.encode()), seed]).standard_normal(out[name].shape)
        drawn = base * np.exp(spread * noise) if base else spread * noise
        out[name] = jnp.asarray(drawn.astype(out[name].dtype))
    for name, factor in factors.items():
        out[name] = (out[name] * factor).astype(out[name].dtype)
    return out
```

```python
import concourse.bass as bass
from concourse import mybir
from contextlib import ExitStack


def cond_resid(nc, x, itok, T, out):
    fp32 = mybir.dt.float32
    i32 = mybir.dt.int32
    ALU = mybir.AluOpType

    B, D, _ = x.shape
    K = T.shape[0]
    P = 128
    Q = 32
    G = P // Q
    N = D // P
    SLOTS = 2

    x_rows = x.rearrange("b (g n q) k -> b g q n k", g=G, q=Q)
    out_rows = out.rearrange("b (g n q) k -> b g q n k", g=G, q=Q)
    T_rows = T.rearrange("t (m n q) (g j) -> t g q m n j", m=G, q=Q, g=G)

    ctx = ExitStack()
    with ctx:
        sb = lambda name, shape, dt: ctx.enter_context(nc.sbuf_tensor(name, shape, dt))
        sem = lambda name: ctx.enter_context(nc.semaphore(name))

        x_sb = [sb(f"x_sb{s}", [P, N, D], fp32) for s in range(SLOTS)]
        T_sb = [sb(f"T_sb{s}", [P, G, N, P], fp32) for s in range(SLOTS)]
        TT = [sb(f"TT{s}", [P, N, N, P], fp32) for s in range(SLOTS)]
        out_sb = [sb(f"out_sb{s}", [P, N, D], fp32) for s in range(SLOTS)]
        tok = sb("tok", [1, B], i32)
        row = sb("row", [1, B], i32)
        wrap = sb("wrap", [1, B], i32)
        prod = [[ctx.enter_context(nc.psum_tensor(f"prod{s}_{n}", [P, D], fp32)) for n in range(N)]
                for s in range(SLOTS)]

        tok_loaded = sem("tok_loaded")
        row_step = sem("row_step")
        T_tile_loaded = [sem(f"T_tile_loaded{n}") for n in range(N)]
        x_tile_loaded = [sem(f"x_tile_loaded{n}") for n in range(N)]
        T_loaded = [sem(f"T_loaded{s}") for s in range(SLOTS)]
        x_loaded = [sem(f"x_loaded{s}") for s in range(SLOTS)]
        TT_ready = sem("TT_ready")
        prod_ready = sem("prod_ready")
        sum_ready = sem("sum_ready")
        stored = [sem(f"stored{s}") for s in range(SLOTS)]
        block = ctx.enter_context(nc.Block())

        ROW_STEPS = 5
        DMA = 16 * G

        @block.sync
        def _(sp):
            def load_T(b, s, tiles, done):
                t = sp.value_load(row[0:1, bass.ds(b, 1)], min_val=0, max_val=K - 1)
                for n0, n1 in tiles:
                    for g in range(G):
                        sp.dma_start(T_sb[s][g * Q:(g + 1) * Q, :, n0:n1],
                                     T_rows[bass.ds(t, 1), g, :, :, n0:n1].rearrange("a q m n j -> (a q) m n j")
                                     ).then_inc(done(n0), 16)

            def load_x(b, s):
                for g in range(G):
                    sp.dma_start(x_sb[s][g * Q:(g + 1) * Q], x_rows[b, g]).then_inc(x_loaded[s], 16)

            sp.dma_start(tok[0:1, :], itok.rearrange("(a b) -> a b", a=1)).then_inc(tok_loaded, 16)
            for n in range(N):
                for g in range(G):
                    sp.dma_start(x_sb[0][g * Q:(g + 1) * Q, n], x_rows[0, g, :, n]).then_inc(x_tile_loaded[n], 16)
            sp.wait_ge(row_step, ROW_STEPS)
            load_T(0, 0, [(n, n + 1) for n in range(N)], lambda n: T_tile_loaded[n])
            load_T(1, 1, [(0, N)], lambda n: T_loaded[1])
            load_x(1, 1)
            with sp.Fori(1, B // SLOTS) as p:
                for s in range(SLOTS):
                    b = p * SLOTS + s
                    sp.wait_ge(TT_ready, (b - SLOTS + 1) * N)
                    load_T(b, s, [(0, N)], lambda n: T_loaded[s])
                    sp.wait_ge(sum_ready, (b - SLOTS + 1) * N)
                    for g in range(G):
                        sp.dma_start(x_sb[s][g * Q:(g + 1) * Q],
                                     x_rows[bass.ds(b, 1), g].rearrange("a q n k -> (a q) n k")
                                     ).then_inc(x_loaded[s], 16)

        @block.scalar
        def _(act):
            with act.Fori(0, B // SLOTS) as p:
                for s in range(SLOTS):
                    b = p * SLOTS + s
                    act.wait_ge(sum_ready, (b + 1) * N)
                    for g in range(G):
                        act.dma_start(out_rows[bass.ds(b, 1), g].rearrange("a q n k -> (a q) n k"),
                                      out_sb[s][g * Q:(g + 1) * Q]).then_inc(stored[s], 16)
            for s in range(SLOTS):
                act.wait_ge(stored[s], DMA * (B // SLOTS))

        @block.vector
        def _(dve):
            dve.wait_ge(tok_loaded, 16)
            nc.vector.tensor_scalar(wrap[:], tok[:], 1.0, float(K), ALU.is_lt, ALU.mult).then_inc(row_step, 1)
            nc.vector.tensor_scalar(row[:], tok[:], 1.0, None, ALU.subtract).then_inc(row_step, 1)
            dve.wait_ge(row_step, 2)
            nc.vector.tensor_tensor(row[:], row[:], wrap[:], ALU.add).then_inc(row_step, 1)
            dve.wait_ge(row_step, 3)
            nc.vector.tensor_scalar(row[:], row[:], 0.0, None, ALU.max).then_inc(row_step, 1)
            dve.wait_ge(row_step, 4)
            nc.vector.tensor_scalar(row[:], row[:], float(K - 1), None, ALU.min).then_inc(row_step, 1)

            def transpose(s, n):
                nc.vector.transpose(TT[s][:, n].rearrange("p j (m r) -> p m j r", r=Q),
                                    T_sb[s][:, :, n].rearrange("p m (j c) -> p m j c", c=Q)).then_inc(TT_ready, 1)

            def add(b, s, n):
                dve.wait_ge(prod_ready, b * N + n + 1)
                nc.vector.tensor_tensor(out_sb[s][:, n], prod[s][n][:], x_sb[s][:, n], ALU.add).then_inc(sum_ready, 1)

            for n in range(N):
                dve.wait_ge(T_tile_loaded[n], DMA)
                transpose(0, n)
            dve.wait_ge(T_loaded[1], DMA)
            for n in range(N):
                transpose(1, n)
            for s in range(SLOTS):
                for n in range(N):
                    add(s, s, n)
            with dve.Fori(1, B // SLOTS) as p:
                for s in range(SLOTS):
                    b = p * SLOTS + s
                    dve.wait_ge(T_loaded[s], DMA * p + (DMA if s else 0))
                    for n in range(N):
                        transpose(s, n)
                for s in range(SLOTS):
                    b = p * SLOTS + s
                    dve.wait_ge(stored[s], DMA * p)
                    for n in range(N):
                        add(b, s, n)

        @block.tensor
        def _(pe):
            def products(b, s, n):
                pe.wait_ge(TT_ready, b * N + n + 1)
                for j in range(N):
                    last = nc.tensor.matmul(prod[s][n][:], TT[s][:, n, j], x_sb[s][:, j],
                                            start=(j == 0), stop=(j == N - 1))
                last.then_inc(prod_ready, 1)

            for n in range(N):
                pe.wait_ge(x_tile_loaded[n], DMA)
            for n in range(N):
                products(0, 0, n)
            pe.wait_ge(x_loaded[1], DMA)
            for n in range(N):
                products(1, 1, n)
            with pe.Fori(1, B // SLOTS) as p:
                for s in range(SLOTS):
                    b = p * SLOTS + s
                    pe.wait_ge(x_loaded[s], DMA * p + (DMA if s else 0))
                    for n in range(N):
                        pe.wait_ge(sum_ready, (b - SLOTS) * N + n + 1)
                        products(b, s, n)


def kernel(x, itok_B_1_98, L0_cond_T):
    import numpy as np
    import concourse.bacc as bacc
    from concourse.bass_utils import run_bass_kernel_spmd

    nc = bacc.Bacc("TRN2", target_bir_lowering=False, num_devices=1)
    arrays, args = {}, []
    for name, a in (("x", x), ("itok", itok_B_1_98), ("T", L0_cond_T)):
        arrays[name] = np.ascontiguousarray(a)
        args.append(nc.dram_tensor(name, arrays[name].shape, mybir.dt.from_np(arrays[name].dtype),
                                   kind="ExternalInput").ap())
    out = nc.dram_tensor("out", arrays["x"].shape, mybir.dt.float32, kind="ExternalOutput").ap()
    cond_resid(nc, *args, out)
    return run_bass_kernel_spmd(nc, [arrays], core_ids=[0]).results[0]["out"]
```

```python
import concourse.bass as bass
from concourse import mybir
from contextlib import ExitStack


def cond_resid(nc, x, itok, T, out):
    fp32 = mybir.dt.float32
    fp32r = mybir.dt.float32r
    i32 = mybir.dt.int32
    ALU = mybir.AluOpType
    COPY = mybir.ActivationFunctionType.Copy

    B, D, _ = x.shape
    K = T.shape[0]
    P = 128
    N = D // P
    S = 2
    TILES = B * N
    AHEAD = 2
    RADIX = 4096.0
    LEAN = 1.0 - 0.5 / RADIX

    x_rows = x.rearrange("b (n p) k -> b p n k", p=P)
    out_rows = out.rearrange("b (n p) k -> b p n k", p=P)
    T_rows = T.rearrange("t (n p) j -> t p n j", p=P)

    ctx = ExitStack()
    with ctx:
        sb = lambda name, shape, dt: ctx.enter_context(nc.sbuf_tensor(name, shape, dt))
        ps = lambda name, shape: ctx.enter_context(nc.psum_tensor(name, shape, fp32))
        sem = lambda name: ctx.enter_context(nc.semaphore(name))

        x_sb = [sb(f"x_sb{s}", [P, N, D], fp32) for s in range(S)]
        T_sb = [sb(f"T_sb{s}", [P, N, D], fp32) for s in range(S)]
        xH = [sb(f"xH{s}", [P, N, D], fp32r) for s in range(S)]
        xL = [sb(f"xL{s}", [P, N, D], fp32r) for s in range(S)]
        xD = [sb(f"xD{s}", [P, N, D], fp32r) for s in range(S)]
        TH = [sb(f"TH{n}", [P, N, P], fp32r) for n in range(N)]
        TrH = [sb(f"TrH{n}", [P, N, P], fp32r) for n in range(N)]
        TrL = [sb(f"TrL{n}", [P, N, P], fp32r) for n in range(N)]
        TD = [sb(f"TD{n}", [P, N, P], fp32r) for n in range(N)]
        rest = [sb(f"rest{i}", [P, D], fp32) for i in range(2)]
        out_sb = [sb(f"out_sb{n}", [P, D], fp32) for n in range(N)]
        eye = sb("eye", [P, P], fp32)
        tok = sb("tok", [1, B], i32)
        row = sb("row", [1, B], i32)
        wrap = sb("wrap", [1, B], i32)
        turned = [ps(f"turned{n}", [P, N, P]) for n in range(N)]
        same = [ps(f"same{i}", [P, D]) for i in range(2)]
        diff = [ps(f"diff{i}", [P, D]) for i in range(2)]

        tok_loaded = sem("tok_loaded")
        row_step = sem("row_step")
        eye_step = sem("eye_step")
        first_T_loaded = [sem(f"first_T_loaded{n}") for n in range(N)]
        T_loaded = [sem(f"T_loaded{s}") for s in range(S)]
        x_loaded = [[sem(f"x_loaded{s}_{n}") for n in range(N)] for s in range(S)]
        T_turned = sem("T_turned")
        TH_ready = sem("TH_ready")
        TrL_ready = sem("TrL_ready")
        TD_ready = sem("TD_ready")
        xH_ready = sem("xH_ready")
        xL_ready = sem("xL_ready")
        xD_ready = sem("xD_ready")
        same_ready = sem("same_ready")
        diff_ready = sem("diff_ready")
        rest_ready = sem("rest_ready")
        sum_ready = sem("sum_ready")
        stored = [sem(f"stored{n}") for n in range(N)]
        block = ctx.enter_context(nc.Block())

        ROW_STEPS = 5

        def batches(eng, step):
            for s in range(S):
                step(s, s, True, False)
            with eng.Fori(1, B // S - 1) as p:
                for s in range(S):
                    step(p * S + s, s, False, False)
            for s in range(S):
                step(B - S + s, s, False, s == S - 1)

        def at_batch(ap, b):
            return ap[b] if isinstance(b, int) else ap[bass.ds(b, 1)].rearrange("a p n k -> (a p) n k")

        @block.sync
        def _(sp):
            def load_x(b, s, n):
                sp.dma_start(x_sb[s][:, n], at_batch(x_rows, b)[:, n]).then_inc(x_loaded[s][n], 16)

            def row_of_T(b):
                return sp.value_load(row[0:1, bass.ds(b, 1)], min_val=0, max_val=K - 1)

            sp.dma_start(tok[0:1, :], itok.rearrange("(a b) -> a b", a=1)).then_inc(tok_loaded, 16)
            load_x(0, 0, 0)
            load_x(0, 0, 1)
            sp.wait_ge(row_step, ROW_STEPS)
            t = row_of_T(0)
            for n in range(2):
                sp.dma_start(T_sb[0][:, n], at_batch(T_rows, t)[:, n]).then_inc(first_T_loaded[n], 16)
            load_x(0, 0, 2)
            load_x(0, 0, 3)
            for n in range(2, N):
                sp.dma_start(T_sb[0][:, n], at_batch(T_rows, t)[:, n]).then_inc(first_T_loaded[n], 16)
            for n in range(N):
                load_x(1, 1, n)
            sp.dma_start(T_sb[1][:], at_batch(T_rows, row_of_T(1))).then_inc(T_loaded[1], 16)

            def step(b, s, first, last):
                ending = isinstance(b, int) and b >= B - S
                for n in range(N):
                    sp.wait_ge(sum_ready, b * N + n + 1)
                    sp.dma_start(at_batch(out_rows, b)[:, n], out_sb[n][:]).then_inc(stored[n], 16)
                    if not ending:
                        load_x(b + S, s, n)
                        if n == 1:
                            sp.wait_ge(T_turned, (b + 1) * N)
                            sp.dma_start(T_sb[s][:], at_batch(T_rows, row_of_T(b + S))).then_inc(T_loaded[s], 16)

            batches(sp, step)
            for n in range(N):
                sp.wait_ge(stored[n], 16 * B)

        @block.scalar
        def _(act):
            def cut_x(b, s, n):
                act.wait_ge(x_loaded[s][n], 16 * (b // S + 1) if isinstance(b, int) else (b - s) * (16 // S) + 16)
                nc.scalar.activation(xH[s][:, n], x_sb[s][:, n], COPY, scale=LEAN).then_inc(xH_ready, 1)

            def cut_T(t, n):
                act.wait_ge(T_turned, t + 1)
                nc.scalar.activation(TH[n][:], turned[n][:], COPY, scale=LEAN)
                nc.scalar.activation(TrH[n][:], turned[n][:], COPY, scale=LEAN * RADIX).then_inc(TH_ready, 1)

            for n in range(N):
                cut_x(0, 0, n)
            for n in range(AHEAD):
                cut_T(n, n)

            def step(b, s, first, last):
                for n in range(N):
                    t = b * N + n
                    if not last:
                        if n == 0 and not (first and s == 0):
                            act.wait_ge(diff_ready, b * N)
                        cut_x(b + 1, (s + 1) % S, n)
                    if not (last and n + AHEAD >= N):
                        cut_T(t + AHEAD, (n + AHEAD) % N)

            batches(act, step)

        @block.gpsimd
        def _(pool):
            nc.gpsimd.memset(eye[:], 0.0).then_inc(eye_step, 1)
            pool.wait_ge(eye_step, 1)
            nc.gpsimd.affine_select(out=eye[:], in_=eye[:], compare_op=ALU.not_equal, fill=1.0,
                                    base=0, pattern=[[-1, P]], channel_multiplier=1).then_inc(eye_step, 1)

            def cut_x(b, s, n):
                pool.wait_ge(xH_ready, b * N + n + 1)
                nc.gpsimd.tensor_tensor(xL[s][:, n], x_sb[s][:, n], xH[s][:, n].bitcast(fp32), ALU.subtract
                                        ).then_inc(xL_ready, 1)

            def cut_T(t, n):
                pool.wait_ge(TrL_ready, t + 1)
                nc.gpsimd.tensor_tensor(TD[n][:], TH[n][:].bitcast(fp32), TrL[n][:].bitcast(fp32), ALU.subtract
                                        ).then_inc(TD_ready, 1)

            for n in range(N):
                cut_x(0, 0, n)
            for n in range(AHEAD):
                cut_T(n, n)

            def step(b, s, first, last):
                for n in range(N):
                    t = b * N + n
                    if not last:
                        cut_x(b + 1, (s + 1) % S, n)
                    if not (last and n + AHEAD >= N):
                        cut_T(t + AHEAD, (n + AHEAD) % N)

            batches(pool, step)

        @block.vector
        def _(dve):
            dve.wait_ge(tok_loaded, 16)
            nc.vector.tensor_scalar(wrap[:], tok[:], 1.0, float(K), ALU.is_lt, ALU.mult).then_inc(row_step, 1)
            nc.vector.tensor_scalar(row[:], tok[:], 1.0, None, ALU.subtract).then_inc(row_step, 1)
            dve.wait_ge(row_step, 2)
            nc.vector.tensor_tensor(row[:], row[:], wrap[:], ALU.add).then_inc(row_step, 1)
            dve.wait_ge(row_step, 3)
            nc.vector.tensor_scalar(row[:], row[:], 0.0, None, ALU.max).then_inc(row_step, 1)
            dve.wait_ge(row_step, 4)
            nc.vector.tensor_scalar(row[:], row[:], float(K - 1), None, ALU.min).then_inc(row_step, 1)

            def cut_x(b, s, n):
                dve.wait_ge(xL_ready, b * N + n + 1)
                nc.vector.scalar_tensor_tensor(xD[s][:, n], xL[s][:, n].bitcast(fp32), -RADIX,
                                               xH[s][:, n].bitcast(fp32), ALU.mult, ALU.add).then_inc(xD_ready, 1)

            def cut_T(t, n):
                dve.wait_ge(TH_ready, t + 1)
                nc.vector.scalar_tensor_tensor(TrL[n][:], turned[n][:], RADIX, TrH[n][:].bitcast(fp32),
                                               ALU.mult, ALU.subtract).then_inc(TrL_ready, 1)

            def sum_up(t, b, s, n, first):
                i = n % 2
                dve.wait_ge(diff_ready, t + 1)
                nc.vector.scalar_tensor_tensor(rest[i][:], diff[i][:], -1.0 / RADIX, x_sb[s][:, n],
                                               ALU.mult, ALU.add).then_inc(rest_ready, 1)
                if not (first and s == 0):
                    dve.wait_ge(stored[n], 16 * b)
                dve.wait_ge(same_ready, t + 1)
                dve.wait_ge(rest_ready, t + 1)
                nc.vector.scalar_tensor_tensor(out_sb[n][:], same[i][:], 1.0 + 1.0 / RADIX, rest[i][:],
                                               ALU.mult, ALU.add).then_inc(sum_ready, 1)

            for n in range(N):
                cut_x(0, 0, n)
            for n in range(AHEAD):
                cut_T(n, n)

            def step(b, s, first, last):
                for n in range(N):
                    t = b * N + n
                    if not (last and n + AHEAD >= N):
                        cut_T(t + AHEAD, (n + AHEAD) % N)
                    if not last:
                        cut_x(b + 1, (s + 1) % S, n)
                    sum_up(t, b, s, n, first)

            batches(dve, step)

        @block.tensor
        def _(pe):
            def turn(t, s, n):
                for j in range(N):
                    last = nc.tensor.transpose(turned[n][:, j], T_sb[s][:, n, j * P:(j + 1) * P], eye[:])
                last.then_inc(T_turned, 1)

            pe.wait_ge(eye_step, 2)
            for n in range(AHEAD):
                pe.wait_ge(first_T_loaded[n], 16)
                turn(n, 0, n)

            def products(t, b, s, n, first):
                i = n % 2
                pe.wait_ge(TH_ready, t + 1)
                if not (first and s == 0 and n < 2):
                    pe.wait_ge(sum_ready, t - 1)
                for j in range(N):
                    if n == 0:
                        pe.wait_ge(xH_ready, b * N + j + 1)
                    nc.tensor.matmul(same[i][:], TH[n][:, j], xH[s][:, j], start=(j == 0), stop=False)
                pe.wait_ge(TrL_ready, t + 1)
                for j in range(N):
                    if n == 0:
                        pe.wait_ge(xL_ready, b * N + j + 1)
                    last = nc.tensor.matmul(same[i][:], TrL[n][:, j], xL[s][:, j], start=False, stop=(j == N - 1))
                last.then_inc(same_ready, 1)
                pe.wait_ge(TD_ready, t + 1)
                for j in range(N):
                    if n == 0:
                        pe.wait_ge(xD_ready, b * N + j + 1)
                    last = nc.tensor.matmul(diff[i][:], TD[n][:, j], xD[s][:, j], start=(j == 0), stop=(j == N - 1))
                last.then_inc(diff_ready, 1)

            def step(b, s, first, last):
                for n in range(N):
                    t = b * N + n
                    m = n + AHEAD
                    if m < N:
                        if first and s == 0:
                            pe.wait_ge(first_T_loaded[m], 16)
                        turn(t + AHEAD, s, m)
                    elif not last:
                        if m == N:
                            nb, ns = b + 1, (s + 1) % S
                            if isinstance(b, int):
                                pe.wait_ge(T_loaded[ns], 16 * (nb // S + (1 if ns else 0)))
                            else:
                                pe.wait_ge(T_loaded[ns], (nb - ns) * (16 // S) + (16 if ns else 0))
                        turn(t + AHEAD, (s + 1) % S, m - N)
                    products(t, b, s, n, first)

            batches(pe, step)


def kernel(x, itok_B_1_98, L0_cond_T):
    import numpy as np
    import concourse.bacc as bacc
    from concourse.bass_utils import run_bass_kernel_spmd

    nc = bacc.Bacc("TRN2", target_bir_lowering=False, num_devices=1)
    arrays, args = {}, []
    for name, a in (("x", x), ("itok", itok_B_1_98), ("T", L0_cond_T)):
        arrays[name] = np.ascontiguousarray(a)
        args.append(nc.dram_tensor(name, arrays[name].shape, mybir.dt.from_np(arrays[name].dtype),
                                   kind="ExternalInput").ap())
    out = nc.dram_tensor("out", arrays["x"].shape, mybir.dt.float32, kind="ExternalOutput").ap()
    cond_resid(nc, *args, out)
    return run_bass_kernel_spmd(nc, [arrays], core_ids=[0]).results[0]["out"]
```

```python
import concourse.bass as bass
from concourse import mybir
from contextlib import ExitStack


def cond_resid(nc, x, itok, T, out):
    fp32 = mybir.dt.float32
    fp32r = mybir.dt.float32r
    ALU = mybir.AluOpType
    COPY = mybir.ActivationFunctionType.Copy

    B, D, _ = x.shape
    K = T.shape[0]
    P = 128
    N = D // P
    S = 2
    Q = 32
    G = P // Q
    AHEAD = 2
    BY_DVE = N - 1
    RADIX = 4096.0
    LEAN = 1.0 - 0.5 / RADIX
    WARM, REWARM = 10, 1

    x_rows = x.rearrange("b (p n) k -> b p n k", n=N)
    out_rows = out.rearrange("b (p n) k -> b p n k", n=N)
    T_rows = T.rearrange("t (p n) j -> t p n j", n=N)
    T_cols = T.rearrange("t (m q n) (g c) -> t n g q m c", q=Q, n=N, g=G)
    itok_row = itok.rearrange("(a b) -> a b", a=1)

    ctx = ExitStack()
    with ctx:
        sb = lambda name, shape, dt: ctx.enter_context(nc.sbuf_tensor(name, shape, dt))
        ps = lambda name, shape: ctx.enter_context(nc.psum_tensor(name, shape, fp32))
        sem = lambda name: ctx.enter_context(nc.semaphore(name))

        x_sb = [sb(f"x_sb{s}", [P, N, D], fp32) for s in range(S)]
        T_sb = [sb(f"T_sb{s}", [P, BY_DVE, D], fp32) for s in range(S)]
        T_cols_sb = [sb(f"T_cols_sb{s}", [P, G, P], fp32) for s in range(S)]
        xH = [sb(f"xH{s}", [P, N, D], fp32r) for s in range(S)]
        xL = [sb(f"xL{s}", [P, N, D], fp32r) for s in range(S)]
        xD = [sb(f"xD{s}", [P, N, D], fp32r) for s in range(S)]
        TH = [sb(f"TH{n}", [P, N, P], fp32r) for n in range(N)]
        TH_r = [sb(f"TH_r{n}", [P, N, P], fp32r) for n in range(N)]
        TL = [sb(f"TL{n}", [P, N, P], fp32r) for n in range(N)]
        TD_r = [sb(f"TD_r{n}", [P, N, P], fp32r) for n in range(N)]
        rest = [sb(f"rest{i}", [P, D], fp32) for i in range(2)]
        out_sb = [sb(f"out_sb{n}", [P, D], fp32) for n in range(N)]
        eye = sb("eye", [P, P], fp32)

        turned_ps = [ps(f"turned_ps{i}", [P, N, P]) for i in range(AHEAD)]
        turned_sb = sb("turned_sb", [P, N, P], fp32)
        turned = [turned_ps[n % AHEAD] for n in range(BY_DVE)] + [turned_sb]
        same = [ps(f"same{i}", [P, D]) for i in range(2)]
        diff = [ps(f"diff{i}", [P, D]) for i in range(2)]
        xH_copy = [ps(f"xH_copy{i}", [P, D]) for i in range(2)]

        eye_step = sem("eye_step")
        x_loaded = [[sem(f"x_loaded{s}_{n}") for n in range(N)] for s in range(S)]
        first_T_loaded = [sem(f"first_T_loaded{n}") for n in range(N)]
        T_loaded = [sem(f"T_loaded{s}") for s in range(S)]
        T_cols_loaded = [sem(f"T_cols_loaded{s}") for s in range(S)]
        turned_by_pe = sem("turned_by_pe")
        turned_by_dve = sem("turned_by_dve")
        TH_ready = sem("TH_ready")
        TL_ready = sem("TL_ready")
        TD_ready = sem("TD_ready")
        xH_ready = sem("xH_ready")
        xH_copied = sem("xH_copied")
        first_xL_ready = [sem(f"first_xL_ready{n}") for n in range(N)]
        xL_ready = sem("xL_ready")
        xD_ready = sem("xD_ready")
        same_ready = sem("same_ready")
        diff_ready = sem("diff_ready")
        rest_ready = sem("rest_ready")
        sum_ready = sem("sum_ready")
        stored = [sem(f"stored{n}") for n in range(N)]
        block = ctx.enter_context(nc.Block())

        def batches(eng, step):
            for s in range(S):
                step(s, s, True, False)
            with eng.Fori(1, B // S - 1) as pair:
                for s in range(S):
                    step(pair * S + s, s, False, False)
            for s in range(S):
                step(B - S + s, s, False, s == S - 1)

        def of(rows, b):
            return rows[b] if isinstance(b, int) else rows[bass.ds(b, 1)].rearrange("a p n k -> (a p) n k")

        def parts_of_tile(last, n):
            h = 2 if last and n == N - 1 else 1
            return [slice(i * D // h, (i + 1) * D // h) for i in range(h)]

        def after(ahead, b, s, n):
            k, n = divmod(n + ahead, N)
            return b + k, (s + k) % S, n

        def beyond(ahead, last, n):
            return last and n + ahead >= N

        def load_x(eng, b, s, n):
            eng.dma_start(x_sb[s][:, n], of(x_rows, b)[:, n]).then_inc(x_loaded[s][n], 16)

        @block.sync
        def _(sp):
            def matrix(b):
                t = sp.value_load(itok_row[0:1, bass.ds(b, 1)]) - 1
                t = t + (t < 0) * K
                t = t * (t > 0)
                t = t + (t > K - 1) * (K - 1 - t)
                return sp.snap(t, min_val=0, max_val=K - 1)

            def load_T_rows(t, s, n0, n1, done):
                sp.dma_start(T_sb[s][:, n0:n1], of(T_rows, t)[:, n0:n1]).then_inc(done, 16)

            def load_T_cols(t, s, done):
                for g in range(G):
                    sp.dma_start(T_cols_sb[s][g * Q:(g + 1) * Q],
                                 T_cols[bass.ds(t, 1), BY_DVE, g].rearrange("a q m c -> (a q) m c")).then_inc(done, 16)

            t = matrix(0)
            for n in range(BY_DVE):
                load_T_rows(t, 0, n, n + 1, first_T_loaded[n])
                if n == 0:
                    load_x(sp, 0, 0, N - 1)
            load_T_cols(t, 0, first_T_loaded[BY_DVE])
            for n in range(N):
                load_x(sp, 1, 1, n)
            t = matrix(1)
            load_T_rows(t, 1, 0, BY_DVE, T_loaded[1])
            load_T_cols(t, 1, T_cols_loaded[1])

            def step(b, s, first, last):
                for n in range(N):
                    for h, k in enumerate(parts_of_tile(last, n)):
                        sp.wait_ge(sum_ready, b * N + n + 1 + h)
                        sp.dma_start(of(out_rows, b)[:, n, k], out_sb[n][:, k]).then_inc(stored[n], 16)
                    if isinstance(b, int) and b >= B - S:
                        continue
                    load_x(sp, b + S, s, n)
                    if n == 1:
                        t = matrix(b + S)
                        sp.wait_ge(turned_by_pe, (b + 1) * BY_DVE)
                        load_T_rows(t, s, 0, BY_DVE, T_loaded[s])
                        sp.wait_ge(turned_by_dve, b + 1)
                        load_T_cols(t, s, T_cols_loaded[s])

            batches(sp, step)
            for n in range(N):
                sp.wait_ge(stored[n], 16 * (B - 1 + len(parts_of_tile(True, n))))

        @block.scalar
        def _(act):
            def cut_x(b, s, n):
                act.wait_ge(x_loaded[s][n], (b - s) * (16 // S) + 16)
                nc.scalar.activation(xH[s][:, n], x_sb[s][:, n], COPY, scale=LEAN).then_inc(xH_ready, 1)

            def cut_T(b, n):
                if n == BY_DVE:
                    act.wait_ge(turned_by_dve, b + 1)
                else:
                    act.wait_ge(turned_by_pe, b * BY_DVE + n + 1)
                nc.scalar.activation(TH_r[n][:], turned[n][:], COPY, scale=LEAN / RADIX)
                nc.scalar.activation(TH[n][:], turned[n][:], COPY, scale=LEAN).then_inc(TH_ready, 1)

            def copy_xH(b, s, n, bank_used):
                act.wait_ge(xH_ready, b * N + n + 1)
                if bank_used:
                    act.wait_ge(xD_ready, b * N + n - 1)
                nc.scalar.activation(xH_copy[n % 2][:], xH[s][:, n].bitcast(fp32), COPY).then_inc(xH_copied, 1)

            for n in range(N - 1):
                load_x(act, 0, 0, n)
            for n in range(N - 1):
                cut_x(0, 0, n)
            cut_T(0, 0)
            cut_x(0, 0, N - 1)
            cut_T(0, 1)

            def step(b, s, first, last):
                for n in range(N):
                    if not last:
                        if n == 0 and not (first and s == 0):
                            act.wait_ge(diff_ready, b * N)
                        cut_x(b + 1, (s + 1) % S, n)
                    if not beyond(AHEAD, last, n):
                        ahead_b, _, m = after(AHEAD, b, s, n)
                        cut_T(ahead_b, m)
                    if not last:
                        copy_xH(b + 1, (s + 1) % S, n, not (first and s == 0 and n < 2))

            batches(act, step)

        @block.gpsimd
        def _(pool):
            nc.gpsimd.memset(eye[:], 0.0).then_inc(eye_step, 1)
            pool.wait_ge(eye_step, 1)
            nc.gpsimd.affine_select(out=eye[:], in_=eye[:], compare_op=ALU.not_equal, fill=1.0,
                                    base=0, pattern=[[-1, P]], channel_multiplier=1).then_inc(eye_step, 1)

            def cut_x(b, s, n, done):
                pool.wait_ge(xH_ready, b * N + n + 1)
                nc.gpsimd.tensor_tensor(xL[s][:, n], x_sb[s][:, n], xH[s][:, n].bitcast(fp32), ALU.subtract
                                        ).then_inc(done, 1)

            def cut_T(b, n):
                pool.wait_ge(TL_ready, b * N + n + 1)
                nc.gpsimd.tensor_tensor(TD_r[n][:], TH_r[n][:].bitcast(fp32), TL[n][:].bitcast(fp32), ALU.subtract
                                        ).then_inc(TD_ready, 1)

            for n in range(0, N, 2):
                cut_x(0, 0, n, first_xL_ready[n])
            for n in range(AHEAD):
                cut_T(0, n)

            def step(b, s, first, last):
                for n in range(N):
                    if not last:
                        cut_x(b + 1, (s + 1) % S, n, xL_ready)
                    if not beyond(AHEAD, last, n):
                        ahead_b, _, m = after(AHEAD, b, s, n)
                        cut_T(ahead_b, m)

            batches(pool, step)

        @block.vector
        def _(dve):
            def first_xL(n):
                dve.wait_ge(xH_ready, n + 1)
                nc.vector.tensor_tensor(xL[0][:, n], x_sb[0][:, n], xH[0][:, n].bitcast(fp32), ALU.subtract
                                        ).then_inc(first_xL_ready[n], 1)

            def first_xD(n):
                dve.wait_ge(first_xL_ready[n], 1)
                nc.vector.scalar_tensor_tensor(xD[0][:, n], xL[0][:, n].bitcast(fp32), -RADIX,
                                               xH[0][:, n].bitcast(fp32), ALU.mult, ALU.add).then_inc(xD_ready, 1)

            def cut_x(b, s, n):
                dve.wait_ge(xL_ready, (b - 1) * N + n + 1)
                dve.wait_ge(xH_copied, (b - 1) * N + n + 1)
                nc.vector.scalar_tensor_tensor(xD[s][:, n], xL[s][:, n].bitcast(fp32), -RADIX, xH_copy[n % 2][:],
                                               ALU.mult, ALU.add).then_inc(xD_ready, 1)

            def cut_T(b, n):
                dve.wait_ge(TH_ready, b * N + n + 1)
                nc.vector.tensor_tensor(TL[n][:], turned[n][:], TH[n][:].bitcast(fp32), ALU.subtract
                                        ).then_inc(TL_ready, 1)

            def turn(b, s, first_T):
                if first_T:
                    dve.wait_ge(first_T_loaded[BY_DVE], 16 * G)
                else:
                    dve.wait_ge(T_cols_loaded[s], (b - s) * (16 * G // S) + 16 * G * s)
                nc.vector.transpose(turned_sb[:].rearrange("p j (m q) -> p m j q", q=Q),
                                    T_cols_sb[s][:].rearrange("p m (c j) -> p m j c", j=N)
                                    ).then_inc(turned_by_dve, 1)

            def sum_up(b, s, n, first, last):
                i = n % 2
                dve.wait_ge(diff_ready, b * N + n + 1)
                nc.vector.tensor_tensor(rest[i][:], x_sb[s][:, n], diff[i][:], ALU.subtract).then_inc(rest_ready, 1)
                if not (first and s == 0):
                    dve.wait_ge(stored[n], 16 * b)
                dve.wait_ge(rest_ready, b * N + n + 1)
                for h, k in enumerate(parts_of_tile(last, n)):
                    dve.wait_ge(same_ready, b * N + n + 1 + h)
                    nc.vector.scalar_tensor_tensor(out_sb[n][:, k], same[(n + h) % 2][:, k], RADIX + 1.0, rest[i][:, k],
                                                   ALU.mult, ALU.add).then_inc(sum_ready, 1)

            first_xL(1)
            first_xD(1)
            first_xD(0)
            first_xD(2)
            cut_T(0, 0)
            first_xL(3)
            cut_T(0, 1)
            first_xD(3)

            def step(b, s, first, last):
                for n in range(N):
                    if n == 0:
                        turn(b, s, first and s == 0)
                    if not beyond(AHEAD, last, n):
                        ahead_b, _, m = after(AHEAD, b, s, n)
                        cut_T(ahead_b, m)
                    sum_first = first and s == 0 and n == 0
                    if sum_first:
                        sum_up(b, s, n, first, last)
                    if not last:
                        cut_x(b + 1, (s + 1) % S, n)
                    if not sum_first:
                        sum_up(b, s, n, first, last)

            batches(dve, step)

        @block.tensor
        def _(pe):
            def warm_up(times):
                for _ in range(times):
                    nc.tensor.matmul(diff[1][:, 0:P], eye[:], eye[:], start=True, stop=True)

            def turn(s, n):
                rows = T_sb[s][:, n].rearrange("p (c j) -> p j c", j=N)
                for j in range(N):
                    done = nc.tensor.transpose(turned[n][:, j], rows[:, j], eye[:])
                done.then_inc(turned_by_pe, 1)

            def turn_ahead(b, s, n, first, last):
                if beyond(AHEAD, last, n):
                    return
                _, ahead_s, m = after(AHEAD, b, s, n)
                if m == BY_DVE:
                    return
                pe.wait_ge(TL_ready, b * N + n + 1)
                if first and s == 0 and n + AHEAD < N:
                    pe.wait_ge(first_T_loaded[m], 16)
                elif m == 0:
                    pe.wait_ge(T_loaded[ahead_s], (b + 1 - ahead_s) * (16 // S) + 16 * ahead_s)
                turn(ahead_s, m)

            def multiply_same(b, s, n, first):
                pe.wait_ge(TH_ready, b * N + n + 1)
                for j in range(N):
                    if n == 0:
                        pe.wait_ge(xH_ready, b * N + j + 1)
                    nc.tensor.matmul(same[n % 2][:], TH_r[n][:, j], xH[s][:, j], start=(j == 0), stop=False)
                pe.wait_ge(TL_ready, b * N + n + 1)
                for j in range(N):
                    if n == 0 and first and s == 0:
                        pe.wait_ge(first_xL_ready[j], 1)
                    elif n == 0:
                        pe.wait_ge(xL_ready, (b - 1) * N + j + 1)
                    done = nc.tensor.matmul(same[n % 2][:], TL[n][:, j], xL[s][:, j], start=False, stop=(j == N - 1))
                done.then_inc(same_ready, 1)

            def multiply_last_same(b, s, n):
                for h, k in enumerate(parts_of_tile(True, n)):
                    if h:
                        pe.wait_ge(sum_ready, b * N + n)
                    pe.wait_ge(TH_ready, b * N + n + 1)
                    pe.wait_ge(TL_ready, b * N + n + 1)
                    bank = same[(n + h) % 2]
                    for j in range(N):
                        nc.tensor.matmul(bank[:, k], TH_r[n][:, j], xH[s][:, j, k], start=(j == 0), stop=False)
                    for j in range(N):
                        done = nc.tensor.matmul(bank[:, k], TL[n][:, j], xL[s][:, j, k], start=False, stop=(j == N - 1))
                    done.then_inc(same_ready, 1)

            def multiply_diff(b, s, n):
                pe.wait_ge(TD_ready, b * N + n + 1)
                for j in range(N):
                    if n == 0:
                        pe.wait_ge(xD_ready, b * N + j + 1)
                    done = nc.tensor.matmul(diff[n % 2][:], TD_r[n][:, j], xD[s][:, j], start=(j == 0),
                                            stop=(j == N - 1))
                done.then_inc(diff_ready, 1)

            pe.wait_ge(eye_step, 2)
            warm_up(WARM)
            for n in range(AHEAD):
                pe.wait_ge(first_T_loaded[n], 16)
                turn(0, n)
                warm_up(REWARM)

            def step(b, s, first, last):
                for n in range(N):
                    if first and s == 0 and n == 0:
                        multiply_same(b, s, n, first)
                        turn_ahead(b, s, n, first, last)
                        multiply_diff(b, s, n)
                        continue
                    turn_ahead(b, s, n, first, last)
                    if not (first and s == 0 and n < 2):
                        pe.wait_ge(sum_ready, b * N + n - 1)
                    if last and n == N - 1:
                        multiply_diff(b, s, n)
                        multiply_last_same(b, s, n)
                    else:
                        multiply_same(b, s, n, first)
                        multiply_diff(b, s, n)

            batches(pe, step)


def kernel(x, itok_B_1_98, L0_cond_T):
    import numpy as np
    import concourse.bacc as bacc
    from concourse.bass_utils import run_bass_kernel_spmd

    nc = bacc.Bacc("TRN2", target_bir_lowering=False, num_devices=1)
    arrays, args = {}, []
    for name, a in (("x", x), ("itok", itok_B_1_98), ("T", L0_cond_T)):
        arrays[name] = np.ascontiguousarray(a)
        args.append(nc.dram_tensor(name, arrays[name].shape, mybir.dt.from_np(arrays[name].dtype),
                                   kind="ExternalInput").ap())
    out = nc.dram_tensor("out", arrays["x"].shape, mybir.dt.float32, kind="ExternalOutput").ap()
    cond_resid(nc, *args, out)
    return run_bass_kernel_spmd(nc, [arrays], core_ids=[0]).results[0]["out"]
```
